# Optimizing a Trainium2 kernel written in Bass

```python
import numpy as np
import jax
import jax.numpy as jnp

def _softmax(x, axis=-1):
    return jax.nn.softmax(x, axis=axis)

def _gelu(x):
    return jax.nn.gelu(x, approximate=True)

def _silu(x):
    return jax.nn.silu(x)

def _sigmoid(x):
    return jax.nn.sigmoid(x)

def _layernorm(x, axis=-1, eps=1e-05):
    m = jnp.mean(x, axis=axis, keepdims=True)
    v = jnp.var(x, axis=axis, keepdims=True)
    return (x - m) / jnp.sqrt(v + eps)

def _scatter_add(tgt, idx, src, axis=0):
    return tgt.at[idx].add(src)

def _segment_sum(src, seg, n):
    return jax.ops.segment_sum(src, seg, n)
kernel_name = 'mk_adj_resnorm_d2_adj_r2_4374d4'

def setup_inputs(seed: int=0):
    np.random.seed(seed)
    _w = jnp.asarray

    def _rec_inputs():
        import jax
        import jax.numpy as jnp
        _gk = jax.random.key(seed)
        x = 7.22e-05 + 1 * jax.random.normal(jax.random.fold_in(_gk, 1), (1354, 512), jnp.float32)
        _a = jax.random.bernoulli(jax.random.fold_in(_gk, 2), 0.0118168, (1354, 1354))
        _a = jnp.logical_or(_a, jnp.eye(1354, dtype=bool))
        _af = _a.astype(jnp.float32)
        _af = _af * jax.random.uniform(jax.random.fold_in(_gk, 3), (1354, 1354), jnp.float32, 0.05, 1)
        adj = _af
        return (x, adj)
    x, adj = _rec_inputs()

    def _L0_gnn_setup():
        import jax, jax.numpy as jnp
        import numpy as np
        N = 4096
        IN_FEATURES = 512
        OUT_FEATURES = 512
        key = jax.random.key(seed)
        k_x, k_adj, k_w, k_b = jax.random.split(key, 4)
        x = jax.random.normal(k_x, (N, IN_FEATURES), dtype=jnp.float32)
        adj = jax.random.uniform(k_adj, (N, N), dtype=jnp.float32)
        stdv = 1.0 / np.sqrt(OUT_FEATURES)
        weight = jax.random.uniform(k_w, (IN_FEATURES, OUT_FEATURES), dtype=jnp.float32, minval=-stdv, maxval=stdv)
        bias = jax.random.uniform(k_b, (OUT_FEATURES,), dtype=jnp.float32, minval=-stdv, maxval=stdv)
        return {'x': x, 'adj': adj, 'weight': weight, 'bias': bias}
    _L0_gnn_all = _L0_gnn_setup()
    _L0_gnn_in = {k: v for k, v in _L0_gnn_all.items() if k in ('weight', 'bias')}
    del _L0_gnn_all

    def _L1_gnn_setup():
        import jax, jax.numpy as jnp
        import numpy as np
        N = 4096
        D = 512

        def adjacent_mat(adj):
            adj = adj + jnp.eye(adj.shape[0], dtype=adj.dtype)
            deg = jnp.sum(adj, axis=1)
            dinv = jnp.where(deg > 0, deg ** (-0.5), 0.0).astype(adj.dtype)
            return dinv[:, None] * adj * dinv[None, :]
        key = jax.random.key(seed)
        k1, k2 = jax.random.split(key)
        x = jax.random.normal(k1, (N, D), dtype=jnp.float32)
        Coefficient2 = 1e-08 * jnp.ones((N, N), dtype=jnp.float32)
        A = jax.random.uniform(k2, (N, N), dtype=jnp.float32)
        return {'x': x, 'Coefficient2': Coefficient2, 'A': A}
    _L1_gnn_all = _L1_gnn_setup()
    _L1_gnn_in = {k: v for k, v in _L1_gnn_all.items() if k in ()}
    del _L1_gnn_all
    return {'x': x, 'adj': adj, 'L0_gnn_weight': _L0_gnn_in['weight'], 'L0_gnn_bias': _L0_gnn_in['bias']}

def reference(x, adj, L0_gnn_weight, L0_gnn_bias):
    import jax
    import jax.numpy as jnp

    def _L0_gnn_ref(x, adj, weight, bias):
        import jax, jax.numpy as jnp
        import numpy as np
        N = 4096
        IN_FEATURES = 512
        OUT_FEATURES = 512
        support = jnp.matmul(x, weight)
        output = jnp.matmul(adj, support)
        return output + bias

    def _L1_gnn_ref(x, Coefficient2, A):
        import jax, jax.numpy as jnp
        import numpy as np
        N = 4096
        D = 512

        def adjacent_mat(adj):
            adj = adj + jnp.eye(adj.shape[0], dtype=adj.dtype)
            deg = jnp.sum(adj, axis=1)
            dinv = jnp.where(deg > 0, deg ** (-0.5), 0.0).astype(adj.dtype)
            return dinv[:, None] * adj * dinv[None, :]
        A_c = jax.lax.stop_gradient(A)
        adj = adjacent_mat((A_c + A_c.T) * 0.5)
        y = Coefficient2 @ adj
        y = y @ x
        return y
    x = _layernorm(x + _L0_gnn_ref(x, adj, L0_gnn_weight, L0_gnn_bias), axis=-1)
    x = _layernorm(x + _L1_gnn_ref(x, adj, adj), axis=-1)
    return x

_drawn_inputs = setup_inputs


def setup_inputs(seed=0):
    import zlib

    import numpy as np

    out = dict(_drawn_inputs(seed))
    spreads = {}
    factors = {}
    for name, (base, spread) in spreads.items():
        noise = np.random.default_rng([zlib.crc32(name.encode()), seed]).standard_normal(out[name].shape)
        drawn = base * np.exp(spread * noise) if base else spread * noise
        out[name] = jnp.asarray(drawn.astype(out[name].dtype))
    for name, factor in factors.items():
        out[name] = (out[name] * factor).astype(out[name].dtype)
    return out
```

```python
from contextlib import ExitStack

import numpy as np

import concourse.bass as bass
from concourse import mybir

F32 = mybir.dt.float32
F32R = mybir.dt.float32r
ALU = mybir.AluOpType
ACT = mybir.ActivationFunctionType
AX = mybir.AxisListType

P = 128
XW, AS, LAP, AZ = range(4)
EPS = 1e-5


def steps(eng, start, stop, head, tail, step):
    for k in range(start, start + head):
        step(k, k // 2, k % 2)
    first = start + head
    with eng.Fori(0, (stop - tail - first) // 2) as t:
        for k0 in (first, first + 1):
            step(t * 2 + k0, t + k0 // 2, k0 % 2)
    for k in range(stop - tail, stop):
        step(k, k // 2, k % 2)


def known(k, low, high):
    return isinstance(k, int) and low <= k < high


def gcn_resnorm(nc, x_rows, x_strips, w, bias, adj_strips, adjt_strips, out):
    NB, _, D = x_rows.shape
    KB = D // P
    SW = NB * P
    assert NB % 2 == 1 and NB >= 5

    def loads_before(phase, par):
        return sum(1 for s in range(NB * phase) if s % 2 == par and s // NB != LAP)

    with ExitStack() as ctx:
        def sb(name, shape, dt=F32):
            return ctx.enter_context(nc.sbuf_tensor(name, shape, dt))

        def sem(name):
            return ctx.enter_context(nc.semaphore(name))

        raw = [sb(f"raw{i}", [P, SW]) for i in range(2)]
        high = [sb(f"high{i}", [P, SW], F32R) for i in range(2)]
        low = [sb(f"low{i}", [P, SW], F32R) for i in range(2)]
        s_high = sb("s_high", [P, NB, D], F32R)
        s_low = sb("s_low", [P, NB, D], F32R)
        x1_high = sb("x1_high", [P, NB, D], F32R)
        x1_low = sb("x1_low", [P, NB, D], F32R)
        w_raw = sb("w_raw", [P, KB, D])
        lap = sb("lap", [P, NB, SW])
        two_eye = sb("two_eye", [P, P])
        row_parts = sb("row_parts", [P, NB, NB])
        deg = sb("deg", [P, NB])
        deg_pos = sb("deg_pos", [P, NB])
        deg_floor = sb("deg_floor", [P, NB])
        deg_root = sb("deg_root", [P, NB])
        deg_recip = sb("deg_recip", [P, NB])
        deg_square = sb("deg_square", [P, NB])
        deg_factor = sb("deg_factor", [P, NB])
        deg_fine = sb("deg_fine", [P, NB])
        dinv = sb("dinv", [P, NB])
        half_dinv = sb("half_dinv", [P, NB])
        bias_sb = sb("bias_sb", [P, D])
        residual = [sb(f"residual{i}", [P, D]) for i in range(2)]
        total = sb("total", [P, D])
        normed = [sb(f"normed{i}", [P, D]) for i in range(2)]
        stats = sb("stats", [P, 6])
        moments = sb("moments", [P, 2])
        var_eps = sb("var_eps", [P, 1])
        std = sb("std", [P, 1])
        rstd0 = sb("rstd0", [P, 1])
        rstd_sq = sb("rstd_sq", [P, 1])
        rstd_fac = sb("rstd_fac", [P, 1])
        rstd = sb("rstd", [P, 1])

        acc = [ctx.enter_context(nc.psum_tensor(f"acc{i}", [P, D], F32)) for i in range(2)]

        w_loaded = [sem(f"w_loaded{i}") for i in range(KB)]
        w_high_ready = sem("w_high_ready")
        w_low_ready = sem("w_low_ready")
        bias_loaded = sem("bias_loaded")
        raw_loaded = [sem(f"raw_loaded{i}") for i in range(2)]
        adj_loaded = [sem(f"adj_loaded{i}") for i in range(2)]
        x_loaded = [sem(f"x_loaded{i}") for i in range(2)]
        high_ready = sem("high_ready")
        low_ready = sem("low_ready")
        step_done = sem("step_done")
        bank_read = sem("bank_read")
        mover_high = sem("mover_high")
        mover_low = sem("mover_low")
        eye_zeroed = sem("eye_zeroed")
        eye_ready = sem("eye_ready")
        diag_added = sem("diag_added")
        lap_added = sem("lap_added")
        lap_summed = sem("lap_summed")
        deg_step = sem("deg_step")
        deg_rooted = sem("deg_rooted")
        dinv_ready = sem("dinv_ready")
        lap_scaled = sem("lap_scaled")
        residual_ready = sem("residual_ready")
        stats_ready = sem("stats_ready")
        moments_ready = sem("moments_ready")
        var_ready = sem("var_ready")
        std_ready = sem("std_ready")
        rstd0_ready = sem("rstd0_ready")
        rstd_sq_ready = sem("rstd_sq_ready")
        rstd_fac_ready = sem("rstd_fac_ready")
        rstd_ready = sem("rstd_ready")
        normed_ready = sem("normed_ready")
        stored = [sem(f"stored{i}") for i in range(2)]

        block = ctx.enter_context(nc.Block())

        @block.sync
        def _(sp):
            def load_raw(phase, k, kpar, source, width):
                par = (NB * phase + kpar) % 2
                sp.dma_start(raw[par][:, 0:width], source[k]).then_inc(raw_loaded[par], 16)

            load_raw(XW, 0, 0, x_strips, D)
            for kb in range(KB):
                sp.dma_start(w_raw[:, kb, :], w[:, kb, :]).then_inc(w_loaded[kb], 16)
            load_raw(XW, 1, 1, x_strips, D)
            sp.dma_start(bias_sb[:, :], bias.to_broadcast([P, D])).then_inc(bias_loaded, 16)
            for k in range(2):
                sp.dma_start(residual[(NB * AS + k) % 2][:, :], x_rows[k]).then_inc(
                    x_loaded[(NB * AS + k) % 2], 16)

            def load_adj_strip(k, half, kpar):
                if not known(k, 0, 2):
                    sp.wait_ge(adj_loaded[kpar], half * 16)
                sp.dma_start(lap[:, k, :], adj_strips[k]).then_inc(adj_loaded[kpar], 16)

            load_adj_strip(0, 0, 0)
            load_adj_strip(1, 0, 1)

            def load_x_strip(k, half, kpar):
                sp.wait_ge(low_ready, k - 1)
                load_raw(XW, k, kpar, x_strips, D)
                load_adj_strip(k, half, kpar)

            steps(sp, 2, NB, 1, 0, load_x_strip)

            def load_adjt_strip(k, _half, kpar):
                sp.wait_ge(low_ready, NB * AS + k - 1)
                if known(k, 2, 3):
                    sp.wait_ge(lap_added, 1)
                load_raw(AS, k, kpar, adjt_strips, SW)

            steps(sp, 0, NB, 3, 0, load_adjt_strip)

            def load_adj_again(k, _half, kpar):
                sp.wait_ge(low_ready, NB * AZ + k - 1)
                load_raw(AZ, k, kpar, adjt_strips, SW)

            steps(sp, 0, NB, 1, 0, load_adj_again)

        @block.gpsimd
        def _(pool):
            pool.memset(two_eye[:, :], 0.0).then_inc(eye_zeroed, 1)
            pool.wait_ge(eye_zeroed, 1)
            pool.affine_select(out=two_eye[:, :], in_=two_eye[:, :], compare_op=ALU.not_equal, fill=2.0,
                               base=0, pattern=[[-1, P]], channel_multiplier=1).then_inc(eye_ready, 1)
            pool.wait_ge(eye_ready, 1)
            pool.wait_ge(bias_loaded, 16)

            def add_bias(k, half, kpar):
                par = (NB * AS + kpar) % 2
                pool.wait_ge(x_loaded[par], half * 16 + 16)
                pool.tensor_tensor(residual[par][:, :], residual[par][:, :], bias_sb[:, :],
                                   ALU.add).then_inc(residual_ready, 1)

            def add_adj(k, half, kpar):
                par = (NB * AS + kpar) % 2
                pool.wait_ge(adj_loaded[kpar], half * 16 + 16)
                diag = lap[:, k, bass.ds(k * P, P)]
                pool.tensor_tensor(diag, diag, two_eye[:, :], ALU.add).then_inc(diag_added, 1)
                pool.wait_ge(diag_added, k + 1)
                pool.wait_ge(raw_loaded[par], (half + 1 + loads_before(AS, par)) * 16)
                pool.tensor_tensor(lap[:, k, :], lap[:, k, :], raw[par][:, :],
                                   ALU.add).then_inc(lap_added, 1)
                if not known(k, 0, 2):
                    add_bias(k - 2, half - 1, kpar)

            steps(pool, 0, NB, 3, 0, add_adj)
            for k in (NB - 2, NB - 1):
                add_bias(k, k // 2, k % 2)

            pool.wait_ge(dinv_ready, 1)
            scale = half_dinv[:, :].unsqueeze(2).to_broadcast([P, NB, P])

            def scale_strip(k, _half, kpar):
                par = (NB * LAP + kpar) % 2
                pool.wait_ge(low_ready, NB * LAP + k - 1)
                pool.tensor_tensor(raw[par][:, :].rearrange("p (j c) -> p j c", c=P),
                                   lap[:, k, :].rearrange("p (j c) -> p j c", c=P),
                                   scale, ALU.mult).then_inc(lap_scaled, 1)

            steps(pool, 0, NB, 1, 0, scale_strip)

            def add_x1(k, _half, kpar):
                par = (NB * AZ + kpar) % 2
                pool.wait_ge(bank_read, NB if known(k, 0, 2) else NB + k - 1)
                pool.tensor_tensor(residual[par][:, :], x1_high[:, k, :].bitcast(F32),
                                   x1_low[:, k, :].bitcast(F32), ALU.add).then_inc(residual_ready, 1)

            pool.wait_ge(mover_low, 2 * NB)
            steps(pool, 0, NB, 3, 0, add_x1)

        def wait_raw(eng, phase, k, half, kpar):
            par = (NB * phase + kpar) % 2
            if phase == LAP:
                eng.wait_ge(lap_scaled, k + 1)
            else:
                eng.wait_ge(raw_loaded[par], (half + 1 + loads_before(phase, par)) * 16)

        def two_on(phase, k, half, kpar):
            if isinstance(k, int) and k + 2 >= NB:
                k = k + 2 - NB
                return phase + 1, k, k // 2, k % 2
            return phase, k + 2, half + 1, kpar

        @block.scalar
        def _(act):
            def split_high(phase, k, half, kpar):
                par = (NB * phase + kpar) % 2
                width = D if phase == XW else SW
                wait_raw(act, phase, k, half, kpar)
                act.activation(high[par][:, 0:width], raw[par][:, 0:width],
                               ACT.Copy).then_inc(high_ready, 1)

            split_high(XW, 0, 0, 0)
            for kb in range(KB):
                act.wait_ge(w_loaded[kb], 16)
                act.activation(x1_high[:, kb, :], w_raw[:, kb, :], ACT.Copy).then_inc(w_high_ready, 1)
            split_high(XW, 1, 0, 1)

            for phase in range(4):
                def step(k, half, kpar):
                    s = k + NB * phase
                    par = (NB * phase + kpar) % 2
                    after = two_on(phase, k, half, kpar)
                    act.wait_ge(step_done, s + 1)
                    if phase == XW:
                        act.activation(s_high[:, k, :], acc[par][:, :], ACT.Copy).then_inc(mover_high, 1)
                    if phase == LAP:
                        act.activation(s_high[:, k, :], acc[par][:, :], ACT.Copy,
                                       scale=dinv[:, bass.ds(k, 1)]).then_inc(mover_high, 1)
                    if after[0] < 4:
                        split_high(*after)
                    if phase in (AS, AZ):
                        run = k + (0 if phase == AS else NB)
                        act.wait_ge(var_ready, run + 1)
                        act.activation(std[:, :], var_eps[:, :], ACT.Sqrt).then_inc(std_ready, 1)
                    if phase == AS:
                        if not known(k, NB - 2, NB):
                            act.dma_start(residual[par][:, :], x_rows[k + 2]).then_inc(x_loaded[par], 16)
                        if known(k, NB - 3, NB - 2):
                            act.wait_ge(deg_step, 3)
                            act.activation(deg_root[:, :], deg_floor[:, :],
                                           ACT.Sqrt).then_inc(deg_rooted, 1)
                        act.wait_ge(normed_ready, k + 1)
                        act.activation(x1_high[:, k, :], normed[par][:, :],
                                       ACT.Copy).then_inc(mover_high, 1)
                    if phase == AZ:
                        act.wait_ge(normed_ready, run + 1)
                        act.dma_start(out[k], normed[par][:, :]).then_inc(stored[par], 16)

                steps(act, 0, NB, 1, 4 if phase == AS else 2, step)

            for par in range(2):
                act.wait_ge(stored[par], 16 * len(range((par - NB * AZ) % 2, NB, 2)))

        @block.vector
        def _(dve):
            def split_low(phase, k, _half, kpar):
                par = (NB * phase + kpar) % 2
                width = D if phase == XW else SW
                dve.wait_ge(high_ready, k + NB * phase + 1)
                if phase == AS and not known(k, 0, 1):
                    dve.wait_ge(lap_added, k + 1)
                dve.tensor_tensor(low[par][:, 0:width], raw[par][:, 0:width],
                                  high[par][:, 0:width].bitcast(F32),
                                  ALU.subtract).then_inc(low_ready, 1)

            split_low(XW, 0, 0, 0)
            for kb in range(KB):
                dve.wait_ge(w_high_ready, kb + 1)
                dve.tensor_tensor(x1_low[:, kb, :], w_raw[:, kb, :], x1_high[:, kb, :].bitcast(F32),
                                  ALU.subtract).then_inc(w_low_ready, 1)
            split_low(XW, 1, 0, 1)

            def sum_rows(k):
                dve.wait_ge(lap_added, k + 1)
                dve.tensor_reduce(row_parts[:, k, :], lap[:, k, :].rearrange("p (j c) -> p j c", c=P),
                                  AX.X, ALU.add).then_inc(lap_summed, 1)

            def degrees():
                dve.wait_ge(lap_summed, NB)
                dve.tensor_reduce(deg[:, :], row_parts[:, :, :].rearrange("p k j -> p j k"), AX.X,
                                  ALU.add).then_inc(deg_step, 1)
                dve.wait_ge(deg_step, 1)
                dve.tensor_scalar(deg_pos[:, :], deg[:, :], 0.0, None, ALU.is_gt).then_inc(deg_step, 1)
                dve.tensor_scalar(deg_floor[:, :], deg[:, :], 0.5, 2.0 ** -116, ALU.mult,
                                  ALU.max).then_inc(deg_step, 1)
                dve.wait_ge(deg_rooted, 1)
                dve.reciprocal(deg_recip[:, :], deg_root[:, :]).then_inc(deg_step, 1)
                dve.wait_ge(deg_step, 4)
                dve.tensor_tensor(deg_square[:, :], deg_recip[:, :], deg_floor[:, :],
                                  ALU.mult).then_inc(deg_step, 1)
                dve.wait_ge(deg_step, 5)
                dve.tensor_tensor(deg_factor[:, :], deg_square[:, :], deg_recip[:, :],
                                  ALU.mult).then_inc(deg_step, 1)
                dve.wait_ge(deg_step, 6)
                dve.tensor_scalar(deg_fine[:, :], deg_factor[:, :], -0.5, 1.5, ALU.mult,
                                  ALU.add).then_inc(deg_step, 1)
                dve.wait_ge(deg_step, 7)
                dve.tensor_tensor(deg_square[:, :], deg_fine[:, :], deg_recip[:, :],
                                  ALU.mult).then_inc(deg_step, 1)
                dve.wait_ge(deg_step, 8)
                dve.tensor_tensor(dinv[:, :], deg_square[:, :], deg_pos[:, :],
                                  ALU.mult).then_inc(deg_step, 1)
                dve.wait_ge(deg_step, 9)
                dve.tensor_scalar(half_dinv[:, :], dinv[:, :], 0.5, None,
                                  ALU.mult).then_inc(dinv_ready, 1)

            for phase in range(4):
                def step(k, half, kpar):
                    s = k + NB * phase
                    par = (NB * phase + kpar) % 2
                    after = two_on(phase, k, half, kpar)
                    last = known(k, NB - 1, NB)
                    if phase in (XW, LAP):
                        dve.wait_ge(mover_high, s + 1)
                        if phase == XW:
                            ins = dve.tensor_tensor(s_low[:, k, :], acc[par][:, :],
                                                    s_high[:, k, :].bitcast(F32), ALU.subtract)
                        else:
                            ins = dve.scalar_tensor_tensor(out=s_low[:, k, :], in0=acc[par][:, :],
                                                           scalar=dinv[:, bass.ds(k, 1)],
                                                           in1=s_high[:, k, :].bitcast(F32),
                                                           op0=ALU.mult, op1=ALU.subtract)
                        ins.then_inc(mover_low, 1)
                        split_low(*after)
                        return

                    run = k + (0 if phase == AS else NB)
                    dve.wait_ge(step_done, s + 1)
                    dve.wait_ge(residual_ready, run + 1)
                    if phase == AZ:
                        dve.wait_ge(normed_ready, run)
                    dve.tensor_tensor(total[:, :], acc[par][:, :], residual[par][:, :],
                                      ALU.add).then_inc(bank_read, 1)
                    dve.wait_ge(bank_read, run + 1)
                    dve.bn_stats(stats[:, :], total[:, :]).then_inc(stats_ready, 1)
                    dve.wait_ge(stats_ready, run + 1)
                    if after[0] < 4 and not last:
                        split_low(*after)
                    dve.bn_aggr(moments[:, :], stats[:, :]).then_inc(moments_ready, 1)
                    dve.wait_ge(moments_ready, run + 1)
                    dve.tensor_scalar(var_eps[:, :], moments[:, 1:2], EPS, None,
                                      ALU.add).then_inc(var_ready, 1)
                    dve.wait_ge(std_ready, run + 1)
                    dve.reciprocal(rstd0[:, :], std[:, :]).then_inc(rstd0_ready, 1)
                    dve.wait_ge(rstd0_ready, run + 1)
                    dve.scalar_tensor_tensor(out=rstd_sq[:, :], in0=var_eps[:, :], scalar=rstd0[:, 0:1],
                                             in1=rstd0[:, :], op0=ALU.mult,
                                             op1=ALU.mult).then_inc(rstd_sq_ready, 1)
                    dve.wait_ge(rstd_sq_ready, run + 1)
                    dve.tensor_scalar(rstd_fac[:, :], rstd_sq[:, :], -0.5, 1.5, ALU.mult,
                                      ALU.add).then_inc(rstd_fac_ready, 1)
                    dve.wait_ge(rstd_fac_ready, run + 1)
                    dve.tensor_tensor(rstd[:, :], rstd_fac[:, :], rstd0[:, :],
                                      ALU.mult).then_inc(rstd_ready, 1)
                    dve.wait_ge(rstd_ready, run + 1)
                    if phase == AZ and not known(k, 0, 2):
                        dve.wait_ge(stored[par], half * 16)
                    dve.tensor_scalar(normed[par][:, :], total[:, :], moments[:, 0:1], rstd[:, 0:1],
                                      ALU.subtract, ALU.mult).then_inc(normed_ready, 1)
                    if phase == AS:
                        if known(k, 0, 1):
                            sum_rows(0)
                            sum_rows(1)
                        if not known(k, NB - 2, NB):
                            sum_rows(k + 2)
                        if known(k, NB - 3, NB - 2):
                            degrees()
                        dve.wait_ge(mover_high, s + 1)
                        dve.tensor_tensor(x1_low[:, k, :], normed[par][:, :],
                                          x1_high[:, k, :].bitcast(F32),
                                          ALU.subtract).then_inc(mover_low, 1)
                    if after[0] < 4 and last:
                        split_low(*after)

                head, tail = {XW: (1, 2), AS: (1, 4), LAP: (1, 2), AZ: (3, 2)}[phase]
                steps(dve, 0, NB, head, tail, step)

        @block.tensor
        def _(pe):
            for phase in range(4):
                movers = (x1_high, x1_low) if phase in (XW, LAP) else (s_high, s_low)
                inner = KB if phase == XW else NB

                def step(k, half, kpar):
                    s = k + NB * phase
                    par = (NB * phase + kpar) % 2
                    pe.wait_ge(low_ready, s + 1)
                    before = phase - 1 if known(k, 0, 2) else phase
                    if before in (XW, LAP):
                        pe.wait_ge(mover_low, s - 1)
                    elif before in (AS, AZ):
                        pe.wait_ge(bank_read, s - 1 - NB * (before + 1) // 2)
                    for j in range(inner):
                        if phase == XW and known(k, 0, 1):
                            pe.wait_ge(w_low_ready, j + 1)
                        if phase != XW and known(k, 0, 1):
                            pe.wait_ge(mover_low, NB * (phase - 1) + j + 1)
                        cols = slice(j * P, (j + 1) * P)
                        pe.matmul(acc[par][:, :], high[par][:, cols], movers[0][:, j, :],
                                  start=(j == 0), stop=False)
                        pe.matmul(acc[par][:, :], high[par][:, cols], movers[1][:, j, :],
                                  start=False, stop=False)
                        product = pe.matmul(acc[par][:, :], low[par][:, cols], movers[0][:, j, :],
                                            start=False, stop=(j == inner - 1))
                    product.then_inc(step_done, 1)

                steps(pe, 0, NB, 3, 0, step)


def kernel(x, adj, L0_gnn_weight, L0_gnn_bias):
    import concourse.bacc as bacc
    from concourse.bass_utils import run_bass_kernel_spmd

    x, adj, w, bias = (np.asarray(a) for a in (x, adj, L0_gnn_weight, L0_gnn_bias))
    n, d = x.shape
    nb, kb = -(-n // P), d // P
    x_pad = np.zeros((nb * P, d), x.dtype)
    x_pad[:n] = x
    adj_pad = np.zeros((nb * P, nb * P), adj.dtype)
    adj_pad[:n, :n] = adj
    rows = adj_pad.reshape(nb, P, nb, P)
    arrays = {
        "x_rows": x_pad.reshape(nb, P, d),
        "x_strips": x_pad.reshape(nb, P, kb, P).transpose(0, 3, 2, 1).reshape(nb, P, kb * P),
        "w": w.reshape(kb, P, d).transpose(1, 0, 2),
        "bias": bias.reshape(1, d),
        "adj_strips": rows.transpose(2, 1, 0, 3).reshape(nb, P, nb * P),
        "adjt_strips": rows.transpose(0, 3, 2, 1).reshape(nb, P, nb * P),
    }
    arrays = {name: np.ascontiguousarray(a) for name, a in arrays.items()}

    nc = bacc.Bacc("TRN2", target_bir_lowering=False, num_devices=1)
    args = [nc.dram_tensor(name, a.shape, mybir.dt.from_np(a.dtype), kind="ExternalInput").ap()
            for name, a in arrays.items()]
    out = nc.dram_tensor("out", (nb, P, d), F32, kind="ExternalOutput").ap()
    gcn_resnorm(nc, *args, out)
    result = run_bass_kernel_spmd(nc, [arrays], core_ids=[0])
    return result.results[0]["out"].reshape(nb * P, d)[:n]
```

```python
from contextlib import ExitStack

import numpy as np

import concourse.bass as bass
from concourse import mybir

F32 = mybir.dt.float32
F32R = mybir.dt.float32r
BF16 = mybir.dt.bfloat16
ALU = mybir.AluOpType
ACT = mybir.ActivationFunctionType
AX = mybir.AxisListType

P = 128
Q = 32
FROM, SPARE = 2 * Q, 3 * Q
XW, AS, LAP, AZ = range(4)
EPS = 1e-5
WARMING = 11
BEFORE_LAST = 4
PIECES = 4


def layout_of_last_block(rows):
    twice = P - rows
    once = rows - twice
    assert 0 < twice <= FROM and 0 < once <= Q
    return twice, once


def steps(eng, start, stop, head, tail, step):
    for k in range(start, start + head):
        step(k, k // 2, k % 2)
    first = start + head
    with eng.Fori(0, (stop - tail - first) // 2) as t:
        for k0 in (first, first + 1):
            step(t * 2 + k0, t + k0 // 2, k0 % 2)
    for k in range(stop - tail, stop):
        step(k, k // 2, k % 2)


def known(k, low, high):
    return isinstance(k, int) and low <= k < high


def gcn_resnorm(nc, n_rows, x_rows, x_strips, w, bias, adj_strips, adjt_strips, diagonals, masks, out):
    NB, _, D = x_rows.shape
    KB = D // P
    SW = NB * P
    LAST = NB - 1
    TWICE, ONCE = layout_of_last_block(n_rows - LAST * P)
    assert NB % 2 == 1 and NB >= 9 and KB * D <= 2 * SW

    def raw_loads(phase, half, kpar):
        par = (NB * phase + kpar) % 2
        before = [s for s in range(NB * phase) if s % 2 == par and s // NB != LAP and s != NB * AS]
        return half + len(before) + (0 if phase == AS and kpar == 0 else 1)

    with ExitStack() as ctx:
        def sb(name, shape, dt=F32):
            return ctx.enter_context(nc.sbuf_tensor(name, shape, dt))

        def sem(name):
            return ctx.enter_context(nc.semaphore(name))

        raw = [sb(f"raw{i}", [P, SW]) for i in range(2)]
        high = [sb(f"high{i}", [P, SW], F32R) for i in range(2)]
        low = [sb(f"low{i}", [P, SW], F32R) for i in range(2)]
        s_high = sb("s_high", [P, NB, D], F32R)
        s_low = sb("s_low", [P, NB, D], F32R)
        x1_high = sb("x1_high", [P, NB, D], F32R)
        x1_low = sb("x1_low", [P, NB, D], F32R)
        x1_last = sb("x1_last", [P, D])
        high_last = sb("high_last", [P, D], F32R)
        lap = sb("lap", [P, NB, SW])
        w_raw = lap[:, NB - 2:NB, :].rearrange("p a b -> p (a b)")[:, 0:KB * D].rearrange(
            "p (k n) -> p k n", k=KB)
        diag_sb = sb("diag_sb", [P, 2, P])
        mask_sb = sb("mask_sb", [P, 2])
        first_here, minus_again = mask_sb[:, 0:1], mask_sb[:, 1:2]
        row_parts = sb("row_parts", [P, NB + 1, NB])
        deg2 = sb("deg2", [P, NB])
        deg_pos = sb("deg_pos", [P, NB])
        deg_quarter = sb("deg_quarter", [P, NB])
        deg_root = sb("deg_root", [P, NB])
        deg_recip = sb("deg_recip", [P, NB])
        deg_fine = sb("deg_fine", [P, NB])
        deg_inv = sb("deg_inv", [P, NB])
        dinv = sb("dinv", [P, NB])
        half_dinv = sb("half_dinv", [P, NB])
        bias_sb = sb("bias_sb", [P, D])
        residual = [sb(f"residual{i}", [P, D]) for i in range(2)]
        total = [sb(f"total{i}", [P, D]) for i in range(2)]
        normed = [sb(f"normed{i}", [P, D]) for i in range(2)]
        quarter_eps = sb("quarter_eps", [P, 1])
        stats = sb("stats", [P, 6])
        moments = sb("moments", [P, 2])
        var_quarter = sb("var_quarter", [P, 1])
        std_half = sb("std_half", [P, 1])
        std_recip = sb("std_recip", [P, 1])
        std = sb("std", [P, 1])
        rstd = sb("rstd", [P, 1])
        shift = sb("shift", [P, 1])
        warm = sb("warm", [P, D], BF16)

        acc = [ctx.enter_context(nc.psum_tensor(f"acc{i}", [P, D], F32)) for i in range(2)]
        warm_bank = ctx.enter_context(nc.psum_tensor("warm_bank", [P, D], F32))

        w_loaded = [sem(f"w_loaded{i}") for i in range(KB)]
        w_high_ready = sem("w_high_ready")
        w_low_ready = sem("w_low_ready")
        constants_loaded = sem("constants_loaded")
        eps_ready = sem("eps_ready")
        warm_ready = sem("warm_ready")
        first_adjt_loaded = sem("first_adjt_loaded")
        raw_loaded = [sem(f"raw_loaded{i}") for i in range(2)]
        adj_loaded = [sem(f"adj_loaded{i}") for i in range(2)]
        x_loaded = [sem(f"x_loaded{i}") for i in range(2)]
        high_ready = sem("high_ready")
        low_ready = sem("low_ready")
        step_done = sem("step_done")
        bank_read = sem("bank_read")
        mover_high = sem("mover_high")
        mover_low = sem("mover_low")
        last_value = sem("last_value")
        y_ready = sem("y_ready")
        diag_added = sem("diag_added")
        lap_added = sem("lap_added")
        lap_summed = sem("lap_summed")
        deg2_ready = sem("deg2_ready")
        deg_quarter_ready = sem("deg_quarter_ready")
        deg_root_ready = sem("deg_root_ready")
        deg_recip_ready = sem("deg_recip_ready")
        deg_fine_ready = sem("deg_fine_ready")
        deg_inv_ready = sem("deg_inv_ready")
        dinv_ready = sem("dinv_ready")
        half_dinv_ready = sem("half_dinv_ready")
        lap_scaled = sem("lap_scaled")
        residual_ready = sem("residual_ready")
        stats_ready = sem("stats_ready")
        moments_ready = sem("moments_ready")
        std_half_ready = sem("std_half_ready")
        std_recip_ready = sem("std_recip_ready")
        std_ready = sem("std_ready")
        rstd_ready = sem("rstd_ready")
        shift_ready = sem("shift_ready")
        normed_ready = sem("normed_ready")
        stored = [sem(f"stored{i}") for i in range(2)]

        block = ctx.enter_context(nc.Block())

        def wait_raw(eng, phase, k, half, kpar):
            par = (NB * phase + kpar) % 2
            if phase == LAP:
                eng.wait_ge(lap_scaled, k + 1)
            elif phase == AS and known(k, 0, 1):
                eng.wait_ge(first_adjt_loaded, 16)
            else:
                eng.wait_ge(raw_loaded[par], raw_loads(phase, half, kpar) * 16)

        def raw_of(phase, k, kpar):
            if phase == AS and known(k, 0, 1):
                return lap[:, LAST, :]
            return raw[(NB * phase + kpar) % 2][:, 0:D if phase == XW else SW]

        @block.sync
        def _(sp):
            def load_raw(phase, k, kpar, source, width):
                par = (NB * phase + kpar) % 2
                sp.dma_start(raw[par][:, 0:width], source[k]).then_inc(raw_loaded[par], 16)

            def load_adj_strip(k, half, kpar):
                if not known(k, 0, 2):
                    sp.wait_ge(adj_loaded[kpar], half * 16)
                sp.dma_start(lap[:, k, :], adj_strips[k]).then_inc(adj_loaded[kpar], 16)

            load_raw(XW, 0, 0, x_strips, D)
            for kb in range(KB):
                sp.dma_start(w_raw[:, kb, :], w[:, kb, :]).then_inc(w_loaded[kb], 16)
            load_raw(XW, 1, 1, x_strips, D)

            def load_x_strip(k, _half, kpar):
                sp.wait_ge(low_ready, k - 1)
                load_raw(XW, k, kpar, x_strips, D)
                if known(k, 2, 3):
                    sp.dma_start(bias_sb[:, :], bias.to_broadcast([P, D])).then_inc(constants_loaded, 16)
                    sp.dma_start(diag_sb[:, :, :], diagonals).then_inc(constants_loaded, 16)
                    sp.dma_start(mask_sb[:, :], masks).then_inc(constants_loaded, 16)
                if known(k, 3, 4):
                    for kx in range(2):
                        par = (NB * AS + kx) % 2
                        sp.dma_start(residual[par][:, :], x_rows[kx]).then_inc(x_loaded[par], 16)
                if known(k, 4, 5):
                    sp.wait_ge(w_low_ready, KB)
                    sp.dma_start(raw_of(AS, 0, 0), adjt_strips[0]).then_inc(first_adjt_loaded, 16)
                if known(k, 5, 7):
                    load_adj_strip(k - 5, 0, k - 5)

            steps(sp, 2, NB, 5, 0, load_x_strip)

            sp.wait_ge(low_ready, NB * AS)
            load_raw(AS, 1, 1, adjt_strips, SW)
            load_adj_strip(2, 1, 0)

            def load_strips_of_adj(k, half, kpar):
                if not known(k, 2, 3):
                    sp.wait_ge(lap_added, k - 1)
                if not known(k, NB - 1, NB):
                    load_adj_strip(k + 1, half + kpar, 1 - kpar)
                sp.wait_ge(low_ready, NB * AS + k - 1)
                load_raw(AS, k, kpar, adjt_strips, SW)

            steps(sp, 2, NB, 2, 1, load_strips_of_adj)

            def load_adjt_again(k, _half, kpar):
                sp.wait_ge(low_ready, NB * AZ + k - 1)
                load_raw(AZ, k, kpar, adjt_strips, SW)

            steps(sp, 0, NB, 1, 0, load_adjt_again)

        @block.gpsimd
        def _(pool):
            pool.memset(quarter_eps[:, :], EPS / 4).then_inc(eps_ready, 1)
            pool.wait_ge(constants_loaded, 48)

            def add_bias(k, half, kpar):
                par = (NB * AS + kpar) % 2
                pool.wait_ge(x_loaded[par], half * 16 + 16)
                pool.tensor_tensor(residual[par][:, :], residual[par][:, :], bias_sb[:, :],
                                   ALU.add).then_inc(residual_ready, 1)

            def add_adj(k, half, kpar):
                if not known(k, 0, 4):
                    add_bias(k - 2, half - 1, kpar)
                pool.wait_ge(adj_loaded[kpar], half * 16 + 16)
                diag = lap[:, k, bass.ds(k * P, P)]
                pool.tensor_tensor(diag, diag, diag_sb[:, 1 if known(k, LAST, NB) else 0, :],
                                   ALU.add).then_inc(diag_added, 1)
                pool.wait_ge(diag_added, k + 1)
                wait_raw(pool, AS, k, half, kpar)
                pool.tensor_tensor(lap[:, k, :], lap[:, k, :], raw_of(AS, k, kpar),
                                   ALU.add).then_inc(lap_added, 1)

            add_bias(0, 0, 0)
            add_bias(1, 0, 1)
            steps(pool, 0, NB, 4, 1, add_adj)
            for k in (NB - 2, NB - 1):
                add_bias(k, k // 2, k % 2)

            pool.wait_ge(half_dinv_ready, 1)
            scale = half_dinv[:, :].unsqueeze(2).to_broadcast([P, NB, P])

            def scale_strip(k, _half, kpar):
                par = (NB * LAP + kpar) % 2
                pool.wait_ge(low_ready, NB * LAP + k - 1)
                pool.tensor_tensor(raw[par][:, :].rearrange("p (j c) -> p j c", c=P),
                                   lap[:, k, :].rearrange("p (j c) -> p j c", c=P),
                                   scale, ALU.mult).then_inc(lap_scaled, 1)

            steps(pool, 0, NB, 1, 0, scale_strip)

            pool.wait_ge(mover_low, 2 * NB)

            def add_x1(k, _half, kpar):
                par = (NB * AZ + kpar) % 2
                pool.wait_ge(bank_read, NB if known(k, 0, 2) else NB + k - 1)
                pool.tensor_tensor(residual[par][:, :], x1_high[:, k, :].bitcast(F32),
                                   x1_low[:, k, :].bitcast(F32), ALU.add).then_inc(residual_ready, 1)

            steps(pool, 0, NB - 1, 2, 0, add_x1)

        def two_on(phase, k, half, kpar):
            if isinstance(k, int) and k + 2 >= NB:
                k = k + 2 - NB
                return phase + 1, k, k // 2, k % 2
            return phase, k + 2, half + 1, kpar

        @block.scalar
        def _(act):
            def split_high(phase, k, half, kpar):
                par = (NB * phase + kpar) % 2
                width = D if phase == XW else SW
                wait_raw(act, phase, k, half, kpar)
                act.activation(high[par][:, 0:width], raw_of(phase, k, kpar),
                               ACT.Copy).then_inc(high_ready, 1)

            split_high(XW, 0, 0, 0)
            for kb in range(KB):
                act.wait_ge(w_loaded[kb], 16)
                act.activation(x1_high[:, kb, :], w_raw[:, kb, :], ACT.Copy).then_inc(w_high_ready, 1)
            split_high(XW, 1, 0, 1)
            act.wait_ge(eps_ready, 1)

            def high_of_last(movers_low, whole, n):
                act.activation(high_last[:, :], whole[:, :], ACT.Copy).then_inc(mover_high, 1)
                act.wait_ge(mover_high, NB * n)
                act.activation(movers_low[0:SPARE, LAST, :], high_last[0:SPARE, :].bitcast(F32), ACT.Copy,
                               scale=mask_sb[0:SPARE, 0:1]).then_inc(y_ready, 1)

            for phase in range(4):
                def step(k, half, kpar):
                    s = k + NB * phase
                    par = (NB * phase + kpar) % 2
                    after = two_on(phase, k, half, kpar)
                    is_last = known(k, LAST, NB)
                    act.wait_ge(step_done, s + 1)
                    if phase in (XW, LAP):
                        scale = dinv[:, bass.ds(k, 1)] if phase == LAP else 1.0
                        if is_last:
                            act.activation(total[par][:, :], acc[par][:, :], ACT.Copy,
                                           scale=scale).then_inc(last_value, 1)
                            act.wait_ge(last_value, 1 if phase == XW else 2)
                            if phase == XW:
                                act.wait_ge(constants_loaded, 48)
                            high_of_last(s_low, total[par], phase + 1)
                        else:
                            act.activation(s_high[:, k, :], acc[par][:, :], ACT.Copy,
                                           scale=scale).then_inc(mover_high, 1)
                    if after[0] < 4 and not (phase == AS and is_last):
                        split_high(*after)
                    if phase in (XW, LAP):
                        return

                    run = k + (0 if phase == AS else NB)
                    act.wait_ge(moments_ready, run + 1)
                    act.activation(std_half[:, :], moments[:, 1:2], ACT.Sqrt, bias=quarter_eps[:, 0:1],
                                   scale=0.25).then_inc(std_half_ready, 1)
                    if phase == AS and not known(k, NB - 2, NB):
                        act.dma_start(residual[par][:, :], x_rows[k + 2]).then_inc(x_loaded[par], 16)
                    act.wait_ge(shift_ready, run + 1)
                    if phase == AZ and not known(k, 0, 2):
                        act.wait_ge(stored[par], half * 16)
                    whole = x1_last if phase == AS and is_last else normed[par]
                    act.activation(whole[:, :], total[par][:, :], ACT.Identity, bias=shift[:, 0:1],
                                   scale=rstd[:, 0:1]).then_inc(normed_ready, 1)
                    act.wait_ge(normed_ready, run + 1)
                    if phase == AZ:
                        act.dma_start(out[k], normed[par][:, :]).then_inc(stored[par], 16)
                        return
                    if is_last:
                        high_of_last(x1_low, whole, phase + 1)
                    else:
                        act.activation(x1_high[:, k, :], whole[:, :], ACT.Copy).then_inc(mover_high, 1)
                    if known(k, NB - 3, NB - 2):
                        act.wait_ge(deg_quarter_ready, 1)
                        act.activation(deg_root[:, :], deg_quarter[:, :],
                                       ACT.Sqrt).then_inc(deg_root_ready, 1)
                    if is_last:
                        split_high(*after)

                head, tail = {XW: (1, 2), AS: (1, 4), LAP: (1, 2), AZ: (3, 2)}[phase]
                steps(act, 0, NB, head, tail, step)

            for par in range(2):
                act.wait_ge(stored[par], 16 * len(range((par - NB * AZ) % 2, NB, 2)))

        @block.vector
        def _(dve):
            dve.memset(warm[:, :], 0.0).then_inc(warm_ready, 1)

            def split_low(phase, k, _half, kpar):
                par = (NB * phase + kpar) % 2
                cut = D if phase == XW else LAST * P
                source = raw_of(phase, k, kpar)
                dve.wait_ge(high_ready, k + NB * phase + 1)
                ins = dve.tensor_tensor(low[par][:, 0:cut], source[:, 0:cut],
                                        high[par][:, 0:cut].bitcast(F32), ALU.subtract)
                if phase != XW:
                    dve.tensor_tensor(low[par][0:SPARE, cut:SW], source[0:SPARE, cut:SW],
                                      high[par][0:SPARE, cut:SW].bitcast(F32), ALU.subtract)
                    ins = dve.tensor_copy(low[par][SPARE:P, cut:SW], high[par][FROM:SPARE, cut:SW].bitcast(F32))
                ins.then_inc(low_ready, 1)

            split_low(XW, 0, 0, 0)
            for kb in range(KB):
                dve.wait_ge(w_high_ready, kb + 1)
                dve.tensor_tensor(x1_low[:, kb, :], w_raw[:, kb, :], x1_high[:, kb, :].bitcast(F32),
                                  ALU.subtract).then_inc(w_low_ready, 1)
            split_low(XW, 1, 0, 1)

            def cut_last(movers, whole, n):
                dve.wait_ge(mover_high, NB * n)
                dve.scalar_tensor_tensor(out=movers[0][:, LAST, :], in0=high_last[:, :].bitcast(F32),
                                         scalar=minus_again, in1=whole[:, :], op0=ALU.mult, op1=ALU.add)
                dve.wait_ge(y_ready, n)
                dve.scalar_tensor_tensor(out=movers[1][SPARE:P, LAST, :], in0=whole[FROM:SPARE, :],
                                         scalar=mask_sb[FROM:SPARE, 0:1],
                                         in1=movers[1][FROM:SPARE, LAST, :].bitcast(F32),
                                         op0=ALU.mult, op1=ALU.subtract).then_inc(mover_low, 1)

            def sum_rows(k, first, stop):
                if first == 0:
                    dve.wait_ge(lap_added, k + 1)
                strip = lap[:, k, first * P:stop * P].rearrange("p (j c) -> p j c", c=P)
                if not known(k, LAST, NB):
                    ins = dve.tensor_reduce(row_parts[:, k, first:stop], strip, AX.X, ALU.add)
                else:
                    dve.tensor_reduce(row_parts[:, LAST, first:stop], strip[:, :, 0:TWICE], AX.X, ALU.add)
                    ins = dve.tensor_reduce(row_parts[:, NB, first:stop],
                                            strip[:, :, FROM:FROM + ONCE], AX.X, ALU.add)
                if stop == NB:
                    ins.then_inc(lap_summed, 1)

            def split_low_x1(k, kpar):
                dve.wait_ge(mover_high, k + NB + 1)
                dve.tensor_tensor(x1_low[:, k, :], normed[(NB * AS + kpar) % 2][:, :],
                                  x1_high[:, k, :].bitcast(F32), ALU.subtract).then_inc(mover_low, 1)

            def degrees():
                dve.wait_ge(lap_summed, NB)
                dve.tensor_reduce(deg2[:, :], row_parts[:, :, :].rearrange("p k j -> p j k"), AX.X,
                                  ALU.add).then_inc(deg2_ready, 1)
                dve.wait_ge(deg2_ready, 1)
                dve.tensor_scalar(deg_quarter[:, :], deg2[:, :], 0.125, 2.0 ** -116, ALU.mult,
                                  ALU.max).then_inc(deg_quarter_ready, 1)
                dve.tensor_scalar(deg_pos[:, :], deg2[:, :], 0.0, None, ALU.is_gt)
                dve.wait_ge(deg_root_ready, 1)
                dve.reciprocal(deg_recip[:, :], deg_root[:, :]).then_inc(deg_recip_ready, 1)
                dve.wait_ge(deg_recip_ready, 1)
                dve.tensor_tensor(deg_fine[:, :], deg_recip[:, :], deg_quarter[:, :],
                                  ALU.mult).then_inc(deg_recip_ready, 1)
                dve.wait_ge(deg_recip_ready, 2)
                dve.tensor_tensor(deg_inv[:, :], deg_fine[:, :], deg_root[:, :],
                                  ALU.add).then_inc(deg_fine_ready, 1)
                dve.wait_ge(deg_fine_ready, 1)
                dve.reciprocal(deg_fine[:, :], deg_inv[:, :]).then_inc(deg_inv_ready, 1)
                dve.wait_ge(deg_inv_ready, 1)
                dve.tensor_tensor(dinv[:, :], deg_fine[:, :], deg_pos[:, :],
                                  ALU.mult).then_inc(dinv_ready, 1)
                dve.wait_ge(dinv_ready, 1)
                dve.tensor_scalar(half_dinv[:, :], dinv[:, :], 0.5, None,
                                  ALU.mult).then_inc(half_dinv_ready, 1)

            for phase in range(4):
                def step(k, half, kpar):
                    s = k + NB * phase
                    par = (NB * phase + kpar) % 2
                    after = two_on(phase, k, half, kpar)
                    is_last = known(k, LAST, NB)
                    if phase in (XW, LAP):
                        dve.wait_ge(mover_high, s + 1)
                        if is_last:
                            if phase == XW:
                                dve.wait_ge(constants_loaded, 48)
                            cut_last((s_high, s_low), total[par], phase + 1)
                        elif phase == XW:
                            dve.tensor_tensor(s_low[:, k, :], acc[par][:, :], s_high[:, k, :].bitcast(F32),
                                              ALU.subtract).then_inc(mover_low, 1)
                        else:
                            dve.scalar_tensor_tensor(out=s_low[:, k, :], in0=acc[par][:, :],
                                                     scalar=dinv[:, bass.ds(k, 1)],
                                                     in1=s_high[:, k, :].bitcast(F32), op0=ALU.mult,
                                                     op1=ALU.subtract).then_inc(mover_low, 1)
                        split_low(*after)
                        if phase == XW and is_last:
                            sum_rows(0, 0, NB)
                            sum_rows(1, 0, NB)
                        return

                    run = k + (0 if phase == AS else NB)

                    def sum_piece(n):
                        if phase == AS and not known(k, NB - 2, NB):
                            sum_rows(k + 2, NB * n // PIECES, NB * (n + 1) // PIECES)

                    dve.wait_ge(step_done, s + 1)
                    if not (phase == AZ and is_last):
                        dve.wait_ge(residual_ready, run + 1)
                    if known(k, 0, 2):
                        dve.wait_ge(mover_low, NB * phase)
                    else:
                        dve.wait_ge(normed_ready, run - 1)
                    added = x1_last if phase == AZ and is_last else residual[par]
                    dve.tensor_tensor(total[par][:, :], acc[par][:, :], added[:, :],
                                      ALU.add).then_inc(bank_read, 1)
                    if phase == AS and not known(k, 0, 1):
                        split_low_x1(k - 1, 1 - kpar)
                    dve.wait_ge(bank_read, run + 1)
                    dve.bn_stats(stats[:, :], total[par][:, :]).then_inc(stats_ready, 1)
                    dve.wait_ge(stats_ready, run + 1)
                    if after[0] < 4 and not is_last:
                        split_low(*after)
                    dve.bn_aggr(moments[:, :], stats[:, :]).then_inc(moments_ready, 1)
                    sum_piece(0)
                    dve.wait_ge(moments_ready, run + 1)
                    dve.tensor_scalar(var_quarter[:, :], moments[:, 1:2], 0.25, EPS / 4, ALU.mult, ALU.add)
                    dve.wait_ge(std_half_ready, run + 1)
                    dve.reciprocal(std_recip[:, :], std_half[:, :]).then_inc(std_recip_ready, 1)
                    sum_piece(1)
                    dve.wait_ge(std_recip_ready, run + 1)
                    dve.scalar_tensor_tensor(out=std[:, :], in0=var_quarter[:, :], scalar=std_recip[:, 0:1],
                                             in1=std_half[:, :], op0=ALU.mult,
                                             op1=ALU.add).then_inc(std_ready, 1)
                    sum_piece(2)
                    dve.wait_ge(std_ready, run + 1)
                    dve.reciprocal(rstd[:, :], std[:, :]).then_inc(rstd_ready, 1)
                    sum_piece(3)
                    dve.wait_ge(rstd_ready, run + 1)
                    dve.tensor_scalar(shift[:, :], moments[:, 0:1], rstd[:, 0:1], -1.0, ALU.mult,
                                      ALU.mult).then_inc(shift_ready, 1)
                    if phase == AS and known(k, NB - 3, NB - 2):
                        degrees()
                    if phase == AS and is_last:
                        cut_last((x1_high, x1_low), x1_last, phase + 1)
                        split_low(*after)

                head, tail = {XW: (1, 2), AS: (1, 4), LAP: (1, 2), AZ: (1, 2)}[phase]
                steps(dve, 0, NB, head, tail, step)

        @block.tensor
        def _(pe):
            pe.wait_ge(warm_ready, 1)
            for i in range(WARMING):
                pe.matmul(warm_bank[:, :], warm[:, 0:P], warm[:, :], start=True, stop=True)

            for phase in range(4):
                movers = (x1_high, x1_low) if phase in (XW, LAP) else (s_high, s_low)
                inner = KB if phase == XW else NB

                def bank_free(k, s):
                    before = phase - 1 if known(k, 0, 2) else phase
                    if before in (XW, LAP):
                        pe.wait_ge(mover_low, s - 1)
                    elif before in (AS, AZ):
                        pe.wait_ge(bank_read, s - 1 - NB * (before + 1) // 2)

                def products(k, kpar, blocks):
                    par = (NB * phase + kpar) % 2
                    for j in blocks:
                        if known(k, 0, 1):
                            if phase == XW:
                                pe.wait_ge(w_low_ready, j + 1)
                            else:
                                pe.wait_ge(mover_low, NB * (phase - 1) + j + 1)
                        cols = slice(j * P, (j + 1) * P)
                        parts = [(high, movers[0]), (high, movers[1]), (low, movers[0])]
                        if phase != XW and j == LAST:
                            parts = [(high, movers[0]), (low, movers[1])]
                        for strip, mover in parts:
                            product = pe.matmul(acc[par][:, :], strip[par][:, cols], mover[:, j, :],
                                                start=(j == 0 and mover is movers[0] and strip is high),
                                                stop=(j == inner - 1 and strip is low))
                    if j == inner - 1:
                        product.then_inc(step_done, 1)

                def step(k, _half, kpar):
                    s = k + NB * phase
                    pe.wait_ge(low_ready, s + 1)
                    bank_free(k, s)
                    products(k, kpar, range(inner))

                if phase != LAP:
                    steps(pe, 0, NB, 3, 0, step)
                else:
                    for k in range(2):
                        pe.wait_ge(low_ready, NB * LAP + k + 1)
                        bank_free(k, NB * LAP + k)
                        products(k, k, range(LAST) if k == 0 else range(BEFORE_LAST))
                    products(0, 0, range(LAST, NB))
                    products(1, 1, range(BEFORE_LAST, NB))
                    steps(pe, 2, NB, 1, 0, step)


def kernel(x, adj, L0_gnn_weight, L0_gnn_bias):
    import concourse.bacc as bacc
    from concourse.bass_utils import run_bass_kernel_spmd

    x, adj, w, bias = (np.asarray(a) for a in (x, adj, L0_gnn_weight, L0_gnn_bias))
    n, d = x.shape
    nb, kb = -(-n // P), d // P
    start = (nb - 1) * P
    twice, once = layout_of_last_block(n - start)
    again = [p for p in range(P) if p >= FROM + once or twice <= p < FROM]
    row = np.arange(nb * P)
    row[start + FROM:start + FROM + once] = np.arange(start + twice, n)
    row[[start + p for p in again]] = np.arange(start, start + twice)
    last = row[start:]
    is_again = np.isin(np.arange(P), again)

    rows = adj[row][:, row].reshape(nb, P, nb, P)
    arrays = {
        "x_rows": x[row].reshape(nb, P, d),
        "x_strips": x[row].reshape(nb, P, kb, P).transpose(0, 3, 2, 1).reshape(nb, P, kb * P),
        "w": w.reshape(kb, P, d).transpose(1, 0, 2),
        "bias": bias.reshape(1, d),
        "adj_strips": rows.transpose(2, 1, 0, 3).reshape(nb, P, nb * P),
        "adjt_strips": rows.transpose(0, 3, 2, 1).reshape(nb, P, nb * P),
        "diagonals": 2 * np.stack([np.eye(P), last[:, None] == last[None, :]], 1).astype(np.float32),
        "masks": np.stack([~is_again, -1 * is_again], 1).astype(np.float32),
    }
    arrays = {name: np.ascontiguousarray(a) for name, a in arrays.items()}

    nc = bacc.Bacc("TRN2", target_bir_lowering=False, num_devices=1)
    args = [nc.dram_tensor(name, a.shape, mybir.dt.from_np(a.dtype), kind="ExternalInput").ap()
            for name, a in arrays.items()]
    out = nc.dram_tensor("out", (nb, P, d), F32, kind="ExternalOutput").ap()
    gcn_resnorm(nc, n, *args, out)
    result = run_bass_kernel_spmd(nc, [arrays], core_ids=[0])
    got = result.results[0]["out"].reshape(nb * P, d)
    return np.concatenate([got[:start + twice], got[start + FROM:start + FROM + once]])
```
